# Optimizing a Trainium2 kernel written in Bass

```python
import numpy as np
import jax
import jax.numpy as jnp

def _softmax(x, axis=-1):
    return jax.nn.softmax(x, axis=axis)

def _gelu(x):
    return jax.nn.gelu(x, approximate=True)

def _silu(x):
    return jax.nn.silu(x)

def _sigmoid(x):
    return jax.nn.sigmoid(x)

def _layernorm(x, axis=-1, eps=1e-05):
    m = jnp.mean(x, axis=axis, keepdims=True)
    v = jnp.var(x, axis=axis, keepdims=True)
    return (x - m) / jnp.sqrt(v + eps)

def _scatter_add(tgt, idx, src, axis=0):
    return tgt.at[idx].add(src)

def _segment_sum(src, seg, n):
    return jax.ops.segment_sum(src, seg, n)
kernel_name = 'mk_cond_resid_d1_seqx_r4_12d635'

def setup_inputs(seed: int=0):
    np.random.seed(seed)
    _w = jnp.asarray

    def _rec_inputs():
        import jax
        import jax.numpy as jnp
        _rk = jax.random.key(seed)
        x = -7.109e-05 + 0.9999 * jax.random.normal(jax.random.fold_in(_rk, 1), (32, 64, 1024), jnp.float32)
        _lenS = 64 - jax.random.randint(jax.random.fold_in(_rk, 7), (32,), 0, max(1, 64 // 4) + 1, jnp.int32)
        _lenS2 = 64 - jax.random.randint(jax.random.fold_in(_rk, 8), (32,), 0, max(1, 64 // 4) + 1, jnp.int32)
        condB_scale = 0.000342416 + 0.0128191 * jax.random.normal(jax.random.fold_in(_rk, 11), (32,), jnp.float32)
        itok_Bx4096x4096_0_255 = jax.random.randint(jax.random.fold_in(_rk, 12), (32, 1024, 1024), 0, 64, jnp.int32)
        condB_wscale = jax.random.uniform(jax.random.fold_in(_rk, 13), (32,), jnp.float32, 0.0, 0.00091742)
        itok_Bx4096_0_255 = jax.random.randint(jax.random.fold_in(_rk, 15), (32, 1024), 0, 64, jnp.int32)
        condB_bscale = jax.random.uniform(jax.random.fold_in(_rk, 16), (32,), jnp.float32, 0.0, 0.000800939)
        return (x, condB_scale, itok_Bx4096x4096_0_255, condB_wscale, itok_Bx4096_0_255, condB_bscale, _lenS)
    x, condB_scale, itok_Bx4096x4096_0_255, condB_wscale, itok_Bx4096_0_255, condB_bscale, _lenS = _rec_inputs()

    def _L0_cond_setup():
        import jax, jax.numpy as jnp
        import numpy as np
        key = jax.random.key(seed)
        ks = jax.random.split(key, 10)
        N, OUT, IN = (8, 1024, 1024)
        B, S = (8, 512)
        return {'x': jax.random.normal(ks[0], (B, S, IN), dtype=jnp.float32), 'weight': jax.random.normal(ks[1], (OUT, IN), dtype=jnp.float32) * 0.02, 'bias': jax.random.normal(ks[2], (OUT,), dtype=jnp.float32) * 0.02, 'scale': jax.random.normal(ks[3], (N,), dtype=jnp.float32) * 0.01, 'wq': jax.random.randint(ks[4], (N, OUT, IN), 0, 64, dtype=jnp.int32), 'wscale': jax.random.uniform(ks[5], (N,), dtype=jnp.float32) * 0.001, 'wzp': jax.random.randint(ks[6], (N,), 0, 64, dtype=jnp.int32), 'bq': jax.random.randint(ks[7], (N, OUT), 0, 64, dtype=jnp.int32), 'bscale': jax.random.uniform(ks[8], (N,), dtype=jnp.float32) * 0.001, 'bzp': jax.random.randint(ks[9], (N,), 0, 64, dtype=jnp.int32)}
    _L0_cond_all = _L0_cond_setup()
    _L0_cond_in = {k: v for k, v in _L0_cond_all.items() if k in ('weight', 'bias')}
    del _L0_cond_all
    return {'x': x, 'condB_scale': condB_scale, 'itok_Bx4096x4096_0_255': itok_Bx4096x4096_0_255, 'condB_wscale': condB_wscale, 'itok_Bx4096_0_255': itok_Bx4096_0_255, 'condB_bscale': condB_bscale, '_lenS': _lenS, 'L0_cond_weight': _L0_cond_in['weight'], 'L0_cond_bias': _L0_cond_in['bias']}

def reference(x, condB_scale, itok_Bx4096x4096_0_255, condB_wscale, itok_Bx4096_0_255, condB_bscale, _lenS, L0_cond_weight, L0_cond_bias):
    import jax
    import jax.numpy as jnp

    def _L0_cond_ref(x, weight, bias, scale, wq, wscale, wzp, bq, bscale, bzp):
        import jax, jax.numpy as jnp
        import numpy as np
        f32 = jnp.float32
        dW = jnp.einsum('i,ijk->jk', scale * wscale, wq.astype(f32)) + jnp.dot(scale, wzp.astype(f32))
        W = weight + dW
        db = jnp.einsum('i,ij->j', scale * bscale, bq.astype(f32)) + jnp.dot(scale, bzp.astype(f32))
        b = bias + db
        return jnp.einsum('bsi,oi->bso', x, W) + b
    x = x + _L0_cond_ref(x, L0_cond_weight, L0_cond_bias, condB_scale, itok_Bx4096x4096_0_255, condB_wscale, _lenS, itok_Bx4096_0_255, condB_bscale, _lenS)
    return x

_drawn_inputs = setup_inputs


def setup_inputs(seed=0):
    import zlib

    import numpy as np

    out = dict(_drawn_inputs(seed))
    spreads = {}
    factors = {'condB_scale': 38.424,
     'condB_wscale': 200.0,
     'condB_bscale': 200.0,
     'L0_cond_weight': 200.0,
     'L0_cond_bias': 200.0}
    for name, (base, spread) in spreads.items():
        noise = np.random.default_rng([zlib.crc32(name.encode()), seed]).standard_normal(out[name].shape)
        drawn = base * np.exp(spread * noise) if base else spread * noise
        out[name] = jnp.asarray(drawn.astype(out[name].dtype))
    for name, factor in factors.items():
        out[name] = (out[name] * factor).astype(out[name].dtype)
    return out
```

```python
from contextlib import ExitStack

import concourse.bass as bass
from concourse import mybir

ALU = mybir.AluOpType
ACT = mybir.ActivationFunctionType
AX = mybir.AxisListType
F32 = mybir.dt.float32
I32 = mybir.dt.int32

P = 128
BANK = 512
RING = 4
X_TILE = 4


def cut(chunks, adapters):
    return [(k0, kc, i0, ni) for k0, kc, ni in chunks for i0 in range(0, adapters, ni)]


def cond_linear_residual(nc: bass.Bass, x, scale, wq, wscale, bq, bscale, zp, weight, bias, out):
    N, OUT, IN = wq.shape
    TOK = x.shape[0] * x.shape[1]
    KT = IN // P
    TT = TOK // P
    QT = BANK // P
    Q = TT // QT
    NB = OUT // P
    TAIL = 2
    MAIN = NB - TAIL
    assert MAIN % 2 == 0 and Q == 4 and N % 32 == 0

    SLOT = 4 * IN
    MAIN_CUT = [(0, IN, SLOT // IN)]
    TAIL_CUTS = [
        [(0, IN // 2, 8), (IN // 2, IN // 2, 8)],
        [(0, 256, 16), (256, 256, 16), (512, 256, 16), (768, 128, 16), (896, 128, 8)],
    ]
    MAIN_TILES = cut(MAIN_CUT, N)
    assert len(MAIN_TILES) % RING == 0

    def block_steps(chunks):
        return 1 + N * len(chunks)

    MAIN_STEPS = block_steps(MAIN_CUT)

    tail_tile, tail_step, tail_chunk = [MAIN * len(MAIN_TILES)], [MAIN * MAIN_STEPS], [MAIN]
    for c in TAIL_CUTS:
        tail_tile.append(tail_tile[-1] + len(cut(c, N)))
        tail_step.append(tail_step[-1] + block_steps(c))
        tail_chunk.append(tail_chunk[-1] + len(c))

    x_rows = x.rearrange("b s k -> (b s) k").rearrange("(p t) k -> p t k", t=TT)
    out_rows = out.rearrange("b s o -> (b s) o").rearrange("(p t) o -> p t o", t=TT)

    ctx = ExitStack()
    with ctx:
        def sb(name, shape, dt=F32):
            return ctx.enter_context(nc.sbuf_tensor(name, shape, dt))

        def sem(name):
            return ctx.enter_context(nc.semaphore(name))

        ring = sb("ring", [P, RING, SLOT], I32)
        xs = sb("xs", [P, X_TILE, IN])
        xT = sb("xT", [P, KT, TOK])
        W = sb("W", [P, 2, IN])
        WT = sb("WT", [P, KT, P])
        yT = sb("yT", [P, Q, BANK])
        y = sb("y", [P, 2, TT, P])
        ident = sb("ident", [P, P])
        scale_all = sb("scale_all", [P, N])
        wscale_all = sb("wscale_all", [P, N])
        zp_all = sb("zp_all", [P, N], I32)
        coef = sb("coef", [P, N])
        zp_terms = sb("zp_terms", [P, N])
        zp_sum = sb("zp_sum", [P, 1])
        bq_rows = sb("bq_rows", [N, OUT], I32)
        bscale_col = sb("bscale_col", [N, 1])
        zp_col = sb("zp_col", [N, 1], I32)
        zp_colf = sb("zp_colf", [N, 1])
        b_rows = sb("b_rows", [N + 1, OUT])
        b_coef = sb("b_coef", [N + 1, 1])
        b_col = sb("b_col", [P, NB])
        b_now = sb("b_now", [P, 2])

        acc = ctx.enter_context(nc.psum_tensor("acc", [P, Q, BANK], F32))
        turn = ctx.enter_context(nc.psum_tensor("turn", [P, 2, KT * P], F32))

        tile_loaded = [sem(f"tile_loaded{s}") for s in range(RING)]
        x_loaded = sem("x_loaded")
        weight_loaded = [sem(f"weight_loaded{s}") for s in range(2)]
        coefs_loaded = sem("coefs_loaded")
        bias_loaded = sem("bias_loaded")
        ident_zeroed = sem("ident_zeroed")
        ident_ready = sem("ident_ready")
        setup = sem("setup")
        b_rows_ready = sem("b_rows_ready")
        b_done = sem("b_done")
        b_ready = sem("b_ready")
        b_now_ready = sem("b_now_ready")
        x_turned = sem("x_turned")
        xT_ready = sem("xT_ready")
        summed = sem("summed")
        w_turned = sem("w_turned")
        WT_ready = sem("WT_ready")
        bank_done = sem("bank_done")
        yT_ready = sem("yT_ready")
        y_turned = sem("y_turned")
        y_ready = sem("y_ready")
        stored = [sem(f"stored{s}") for s in range(2)]

        block = ctx.enter_context(nc.Block())

        def tile_view(s, kc, ni):
            return ring[:, s, 0:ni * kc].rearrange("p (i k) -> p i k", i=ni)

        def last_step(tiles, j):
            return 1 + sum(ni for _, _, _, ni in tiles[:j + 1])

        @block.sync
        def _(sp):
            def load_tile(row, tiles, j, s):
                k0, kc, i0, ni = tiles[j]
                sp.dma_start(tile_view(s, kc, ni),
                             wq[i0:i0 + ni, bass.ds(row, P), k0:k0 + kc].rearrange("i p k -> p i k")
                             ).then_inc(tile_loaded[s], 16)

            for j in range(len(MAIN_TILES)):
                if j >= RING:
                    sp.wait_ge(summed, last_step(MAIN_TILES, j - RING))
                load_tile(0, MAIN_TILES, j, j % RING)
                if j % 2:
                    n = j // 2
                    if n:
                        sp.wait_ge(x_turned, n * X_TILE)
                    sp.dma_start(xs[:, :, :], x_rows[:, n * X_TILE:(n + 1) * X_TILE, :]
                                 ).then_inc(x_loaded, 16)
            with sp.Fori(1, MAIN) as b:
                for j in range(len(MAIN_TILES)):
                    if j >= RING:
                        sp.wait_ge(summed, b * MAIN_STEPS + last_step(MAIN_TILES, j - RING))
                    else:
                        sp.wait_ge(summed, b * MAIN_STEPS - MAIN_STEPS
                                   + last_step(MAIN_TILES, len(MAIN_TILES) - RING + j))
                    load_tile(b * P, MAIN_TILES, j, j % RING)
            used = [(MAIN - 1) * MAIN_STEPS + last_step(MAIN_TILES, j) for j in range(len(MAIN_TILES))]
            for n, chunks in enumerate(TAIL_CUTS):
                tiles = cut(chunks, N)
                for j in range(len(tiles)):
                    g = tail_tile[n] + j
                    sp.wait_ge(summed, used[len(used) - RING])
                    load_tile((MAIN + n) * P, tiles, j, g % RING)
                    used.append(tail_step[n] + last_step(tiles, j))
            last = NB - 1
            for q in range(Q):
                sp.wait_ge(y_ready, last * Q + q + 1)
                sp.dma_start(out_rows[:, q * QT:(q + 1) * QT, last * P:(last + 1) * P],
                             y[:, last % 2, q * QT:(q + 1) * QT, :]).then_inc(stored[last % 2], 16)
            sp.wait_ge(stored[0], 16 * (NB // 2))
            sp.wait_ge(stored[1], 16 * (NB // 2 - 1 + Q))

        @block.gpsimd
        def _(pool):
            nc.gpsimd.memset(ident[:, :], 0.0).then_inc(ident_zeroed, 1)
            pool.wait_ge(ident_zeroed, 1)
            nc.gpsimd.affine_select(out=ident[:, :], in_=ident[:, :], compare_op=ALU.not_equal, fill=1.0,
                                    base=0, pattern=[[-1, P]], channel_multiplier=1).then_inc(ident_ready, 1)

        @block.vector
        def _(dve):
            dve.wait_ge(coefs_loaded, 3 * 16)
            nc.vector.tensor_tensor(coef[:, :], scale_all[:, :], wscale_all[:, :], ALU.mult).then_inc(setup, 1)
            nc.vector.tensor_tensor(zp_terms[:, :], scale_all[:, :], zp_all[:, :], ALU.mult).then_inc(setup, 1)
            dve.wait_ge(setup, 2)
            nc.vector.reduce_sum(zp_sum[:, :], zp_terms[:, :], axis=AX.X).then_inc(setup, 1)
            dve.wait_ge(bias_loaded, 5 * 16)
            nc.vector.memset(b_coef[N:N + 1, :], 1.0).then_inc(b_rows_ready, 1)
            nc.vector.tensor_copy(zp_colf[:, :], zp_col[:, :]).then_inc(setup, 1)
            dve.wait_ge(setup, 4)
            nc.vector.tensor_scalar(b_rows[0:N, :], bq_rows[:, :], bscale_col[:, 0:1], zp_colf[:, 0:1],
                                    ALU.mult, ALU.add).then_inc(b_rows_ready, 1)
            dve.wait_ge(ident_ready, 1)

            def sum_block(par, loads, block_index, first_step, uses, tiles):
                dve.wait_ge(weight_loaded[par], 16 * loads)
                diag = W[:, par, bass.ds(block_index * P, P)]
                nc.vector.tensor_tensor(diag, diag, ident[:, :], ALU.add).then_inc(summed, 1)
                step = 1
                for j, (k0, kc, i0, ni) in enumerate(tiles):
                    s, use = uses(j)
                    dve.wait_ge(tile_loaded[s], 16 * use)
                    part = W[:, par, k0:k0 + kc]
                    for i in range(ni):
                        dve.wait_ge(summed, first_step + step)
                        nc.vector.scalar_tensor_tensor(
                            out=part, in0=tile_view(s, kc, ni)[:, i, :], scalar=coef[:, i0 + i:i0 + i + 1],
                            in1=part, op0=ALU.mult, op1=ALU.add).then_inc(summed, 1)
                        step += 1

            rounds = len(MAIN_TILES) // RING
            with dve.Fori(0, MAIN // 2) as pair:
                for par in range(2):
                    b = pair * 2 + par
                    sum_block(par, pair + 1, b, b * MAIN_STEPS,
                              lambda j, b=b: (j % RING, b * rounds + (j // RING + 1)), MAIN_TILES)
            for n, chunks in enumerate(TAIL_CUTS):
                b = MAIN + n
                sum_block(b % 2, b // 2 + 1, b, tail_step[n],
                          lambda j, n=n: ((tail_tile[n] + j) % RING, (tail_tile[n] + j) // RING + 1),
                          cut(chunks, N))
            last = NB - 1
            dve.wait_ge(stored[last % 2], 16 * (last // 2))
            for q in range(Q):
                dve.wait_ge(y_turned, last * Q + q + 1)
                nc.vector.tensor_copy(y[:, last % 2, q * QT:(q + 1) * QT, :],
                                      acc[:, q, :].rearrange("p (t o) -> p t o", o=P)).then_inc(y_ready, 1)

        @block.tensor
        def _(pe):
            pe.wait_ge(b_rows_ready, 2)
            for n in range(NB):
                mm = nc.tensor.matmul(acc[:, 0, n:n + 1], b_rows[:, n * P:(n + 1) * P], b_coef[:, :],
                                      start=True, stop=True)
            mm.then_inc(b_done, 1)
            pe.wait_ge(ident_ready, 1)
            for t in range(TT):
                if t % X_TILE == 0:
                    pe.wait_ge(x_loaded, 16 * (t // X_TILE + 1))
                if t >= 2:
                    pe.wait_ge(xT_ready, t - 1)
                for k in range(KT):
                    mm = nc.tensor.transpose(turn[:, t % 2, k * P:(k + 1) * P],
                                             xs[:, t % X_TILE, k * P:(k + 1) * P], ident[:, :])
                mm.then_inc(x_turned, 1)
            pe.wait_ge(xT_ready, TT)
            pe.wait_ge(b_ready, 1)

            def turn_back(q, b):
                pe.wait_ge(yT_ready, b * Q + q + 1)
                for t in range(QT):
                    mm = nc.tensor.transpose(acc[:, q, t * P:(t + 1) * P], yT[:, q, t * P:(t + 1) * P],
                                             ident[:, :])
                mm.then_inc(y_turned, 1)

            def product_block(par, b, first_step, first_chunk, chunks, first):
                for c, (k0, kc, _) in enumerate(chunks):
                    pe.wait_ge(summed, first_step + 1 + N * (c + 1))
                    k_tiles = range(k0 // P, (k0 + kc) // P)
                    for k in k_tiles:
                        mm = nc.tensor.transpose(turn[:, 0, k * P:(k + 1) * P],
                                                 W[:, par, k * P:(k + 1) * P], ident[:, :])
                    mm.then_inc(w_turned, 1)
                    pe.wait_ge(WT_ready, first_chunk + c + 1)
                    for q in range(Q):
                        if c == 0 and not first:
                            pe.wait_ge(y_ready, b * Q - Q + q + 1)
                        for k in k_tiles:
                            mm = nc.tensor.matmul(acc[:, q, :], WT[:, k, :], xT[:, k, q * BANK:(q + 1) * BANK],
                                                  start=(k == 0), stop=(k == KT - 1))
                        if c == len(chunks) - 1:
                            mm.then_inc(bank_done, 1)
                            if q:
                                turn_back(q - 1, b)
                turn_back(Q - 1, b)

            product_block(0, 0, 0, 0, MAIN_CUT, True)
            product_block(1, 1, MAIN_STEPS, 1, MAIN_CUT, False)
            with pe.Fori(1, MAIN // 2) as pair:
                for par in range(2):
                    b = pair * 2 + par
                    product_block(par, b, b * MAIN_STEPS, b, MAIN_CUT, False)
            for n, chunks in enumerate(TAIL_CUTS):
                b = MAIN + n
                product_block(b % 2, b, tail_step[n], tail_chunk[n], chunks, False)

        @block.scalar
        def _(act):
            def load_weight(row, par):
                act.dma_start(W[:, par, :], weight[bass.ds(row, P), :]).then_inc(weight_loaded[par], 16)

            def everywhere(v):
                return v.rearrange("(a n) -> a n", a=1).to_broadcast([P, N])

            def column(v):
                return v.rearrange("(n a) -> n a", a=1)

            act.dma_start(scale_all[:, :], everywhere(scale)).then_inc(coefs_loaded, 16)
            act.dma_start(wscale_all[:, :], everywhere(wscale)).then_inc(coefs_loaded, 16)
            act.dma_start(zp_all[:, :], everywhere(zp)).then_inc(coefs_loaded, 16)
            load_weight(0, 0)
            act.dma_start(b_coef[0:N, :], column(scale)).then_inc(bias_loaded, 16)
            act.dma_start(bscale_col[:, :], column(bscale)).then_inc(bias_loaded, 16)
            act.dma_start(zp_col[:, :], column(zp)).then_inc(bias_loaded, 16)
            act.dma_start(bq_rows[:, :], bq).then_inc(bias_loaded, 16)
            act.dma_start(b_rows[N:N + 1, :], bias.rearrange("(a n) -> a n", a=1)).then_inc(bias_loaded, 16)
            load_weight(P, 1)

            act.wait_ge(b_done, 1)
            nc.scalar.copy(b_col[:, :], acc[:, 0, 0:NB]).then_inc(b_ready, 1)
            for t in range(TT):
                act.wait_ge(x_turned, t + 1)
                nc.scalar.copy(xT[:, :, t * P:(t + 1) * P],
                               turn[:, t % 2, :].rearrange("k (j p) -> k j p", p=P)).then_inc(xT_ready, 1)
            act.wait_ge(setup, 3)

            def finish_block(par, b, first_chunk, chunks, stores):
                for c, (k0, kc, _) in enumerate(chunks):
                    act.wait_ge(w_turned, first_chunk + c + 1)
                    if c == len(chunks) - 1 and stores is not None:
                        stores()
                    nc.scalar.activation(WT[:, k0 // P:(k0 + kc) // P, :],
                                         turn[:, 0, k0:k0 + kc].rearrange("k (j p) -> k j p", p=P),
                                         ACT.Identity, bias=zp_sum[:, 0:1]).then_inc(WT_ready, 1)

            def pick_bias(b, par):
                nc.scalar.copy(b_now[:, par:par + 1], b_col[:, bass.ds(b, 1)]).then_inc(b_now_ready, 1)

            def take_product(q, b, par):
                act.wait_ge(bank_done, b * Q + q + 1)
                nc.scalar.activation(yT[:, q, :], acc[:, q, :], ACT.Identity,
                                     bias=b_now[:, par:par + 1]).then_inc(yT_ready, 1)

            def take_result(q, b, par):
                act.wait_ge(y_turned, b * Q + q + 1)
                nc.scalar.copy(y[:, par, q * QT:(q + 1) * QT, :],
                               acc[:, q, :].rearrange("p (t o) -> p t o", o=P)).then_inc(y_ready, 1)

            def results_and_store(par, b, earlier_stores):
                pick_bias(b, par)
                act.wait_ge(b_now_ready, b + 1)
                if earlier_stores is not None:
                    act.wait_ge(stored[par], earlier_stores)
                take_product(0, b, par)
                for q in range(1, Q):
                    take_product(q, b, par)
                    take_result(q - 1, b, par)
                take_result(Q - 1, b, par)
                act.wait_ge(y_ready, b * Q + Q)
                act.dma_start(out_rows[:, :, bass.ds(b * P, P)], y[:, par, :, :]).then_inc(stored[par], 16)

            def main_block(par, b, earlier_stores):
                finish_block(par, b, b, MAIN_CUT, lambda: load_weight(b * P + 2 * P, par))
                results_and_store(par, b, earlier_stores)

            for par in range(2):
                main_block(par, par, None)
            with act.Fori(1, MAIN // 2) as pair:
                for par in range(2):
                    main_block(par, pair * 2 + par, pair * 16)
            for n, chunks in enumerate(TAIL_CUTS):
                b = MAIN + n
                finish_block(b % 2, b, tail_chunk[n], chunks, None)
                if b < NB - 1:
                    results_and_store(b % 2, b, 16 * (b // 2))
            pick_bias(NB - 1, (NB - 1) % 2)
            act.wait_ge(b_now_ready, NB)
            for q in range(Q):
                take_product(q, NB - 1, (NB - 1) % 2)


_INS = ['x', 'condB_scale', 'itok_Bx4096x4096_0_255', 'condB_wscale', 'itok_Bx4096_0_255', 'condB_bscale',
        '_lenS', 'L0_cond_weight', 'L0_cond_bias']
_OUTS = [((32, 64, 1024), 'float32')]


def kernel(**inputs):
    import numpy as _np
    import concourse.bacc as _bacc
    from concourse import mybir as _mybir
    from concourse.bass_utils import run_bass_kernel_spmd as _run

    nc = _bacc.Bacc("TRN2", target_bir_lowering=False, num_devices=1)
    arrays, args = {}, []
    for name in _INS:
        a = _np.ascontiguousarray(inputs[name])
        arrays[f"in_{name}_dram"] = a
        args.append(nc.dram_tensor(f"in_{name}_dram", a.shape, _mybir.dt.from_np(a.dtype), kind="ExternalInput").ap())
    for i, (shape, dtype) in enumerate(_OUTS):
        dt = _mybir.dt.from_np(_np.dtype(dtype))
        args.append(nc.dram_tensor(f"out_{i}_dram", shape, dt, kind="ExternalOutput").ap())
    cond_linear_residual(nc, *args)
    r = _run(nc, [arrays], core_ids=[0])
    got = tuple(r.results[0][f"out_{i}_dram"] for i in range(len(_OUTS)))
    return got[0]
```

```python
from contextlib import ExitStack

import concourse.bass as bass
from concourse import mybir

ALU = mybir.AluOpType
ACT = mybir.ActivationFunctionType
AX = mybir.AxisListType
F32 = mybir.dt.float32
I32 = mybir.dt.int32

P = 128
BANK = 512
RING = 4
X_TILE = 4


def cut(chunks, adapters):
    return [(k0, kc, i0, ni) for k0, kc, ni in chunks for i0 in range(0, adapters, ni)]


def cond_linear_residual(nc: bass.Bass, x, scale, wq, wscale, bq, bscale, zp, weight, bias, out):
    N, OUT, IN = wq.shape
    TOK = x.shape[0] * x.shape[1]
    KT = IN // P
    TT = TOK // P
    QT = BANK // P
    Q = TT // QT
    NB = OUT // P
    TAIL = 2
    MAIN = NB - TAIL
    assert MAIN % 2 == 0 and Q == 4 and N % 32 == 0

    SLOT = 4 * IN
    MAIN_CUT = [(0, IN, SLOT // IN)]
    TAIL_CUTS = [
        [(0, IN // 2, 8), (IN // 2, IN // 2, 8)],
        [(0, IN // 2, 8), (IN // 2, IN // 4, 8), (3 * IN // 4, IN // 4, 4)],
    ]
    MAIN_TILES = cut(MAIN_CUT, N)
    assert len(MAIN_TILES) % RING == 0

    MAIN_STEPS = 1 + N
    TAIL_CHUNK_STEPS = N + 1

    tail_tile, tail_step, tail_chunk = [MAIN * len(MAIN_TILES)], [MAIN * MAIN_STEPS], [MAIN]
    for c in TAIL_CUTS:
        tail_tile.append(tail_tile[-1] + len(cut(c, N)))
        tail_step.append(tail_step[-1] + 1 + TAIL_CHUNK_STEPS * len(c))
        tail_chunk.append(tail_chunk[-1] + len(c))

    x_rows = x.rearrange("b s k -> (b s) k").rearrange("(p t) k -> p t k", t=TT)
    out_rows = out.rearrange("b s o -> (b s) o").rearrange("(p t) o -> p t o", t=TT)

    ctx = ExitStack()
    with ctx:
        def sb(name, shape, dt=F32):
            return ctx.enter_context(nc.sbuf_tensor(name, shape, dt))

        def sem(name):
            return ctx.enter_context(nc.semaphore(name))

        ring = sb("ring", [P, RING, SLOT], I32)
        xs = sb("xs", [P, X_TILE, IN])
        xT = sb("xT", [P, KT, TOK])
        W = sb("W", [P, 2, IN])
        odd = sb("odd", [P, IN // 2])
        WT = sb("WT", [P, KT, P])
        yT = sb("yT", [P, Q, BANK])
        y = sb("y", [P, 2, TT, P])
        ident = sb("ident", [P, P])
        scale_all = sb("scale_all", [P, N])
        wscale_all = sb("wscale_all", [P, N])
        zp_all = sb("zp_all", [P, N], I32)
        coef = sb("coef", [P, N])
        zp_terms = sb("zp_terms", [P, N])
        zp_sum = sb("zp_sum", [P, 1])
        bq_rows = sb("bq_rows", [N, OUT], I32)
        bscale_col = sb("bscale_col", [N, 1])
        zp_col = sb("zp_col", [N, 1], I32)
        zp_colf = sb("zp_colf", [N, 1])
        b_rows = sb("b_rows", [N + 1, OUT])
        b_coef = sb("b_coef", [N + 1, 1])
        b_col = sb("b_col", [P, NB])
        b_now = sb("b_now", [P, 2])

        acc = ctx.enter_context(nc.psum_tensor("acc", [P, Q, BANK], F32))
        turn = ctx.enter_context(nc.psum_tensor("turn", [P, 2, KT * P], F32))

        tile_loaded = [sem(f"tile_loaded{s}") for s in range(RING)]
        x_loaded = sem("x_loaded")
        weight_loaded = [sem(f"weight_loaded{s}") for s in range(2)]
        coefs_loaded = sem("coefs_loaded")
        bias_loaded = sem("bias_loaded")
        ident_zeroed = sem("ident_zeroed")
        ident_ready = sem("ident_ready")
        setup = sem("setup")
        b_rows_ready = sem("b_rows_ready")
        b_done = sem("b_done")
        b_ready = sem("b_ready")
        b_now_ready = sem("b_now_ready")
        x_turned = sem("x_turned")
        xT_ready = sem("xT_ready")
        summed = sem("summed")
        w_turned = sem("w_turned")
        WT_ready = sem("WT_ready")
        bank_done = sem("bank_done")
        yT_ready = sem("yT_ready")
        y_turned = sem("y_turned")
        y_ready = sem("y_ready")
        last_stored = sem("last_stored")
        stored = [sem(f"stored{s}") for s in range(2)]

        block = ctx.enter_context(nc.Block())

        y_last = xs[:, :, :].rearrange("p a b -> p (a b)")[:, 0:TT * P].rearrange("p (t o) -> p t o", o=P)

        def tile_view(s, kc, ni):
            return ring[:, s, 0:ni * kc].rearrange("p (i k) -> p i k", i=ni)

        def last_step(tiles, j, tail=False):
            added_up = sum(i0 + ni == N for _, _, i0, ni in tiles[:j]) if tail else 0
            return 1 + sum(ni for _, _, _, ni in tiles[:j + 1]) + added_up

        @block.sync
        def _(sp):
            def load_tile(row, tiles, j, s):
                k0, kc, i0, ni = tiles[j]
                sp.dma_start(tile_view(s, kc, ni),
                             wq[i0:i0 + ni, bass.ds(row, P), k0:k0 + kc].rearrange("i p k -> p i k")
                             ).then_inc(tile_loaded[s], 16)

            def everywhere(v):
                return v.rearrange("(a n) -> a n", a=1).to_broadcast([P, N])

            def column(v):
                return v.rearrange("(n a) -> n a", a=1)

            sp.dma_start(scale_all[:, :], everywhere(scale)).then_inc(coefs_loaded, 16)
            sp.dma_start(wscale_all[:, :], everywhere(wscale)).then_inc(coefs_loaded, 16)
            sp.dma_start(zp_all[:, :], everywhere(zp)).then_inc(coefs_loaded, 16)
            sp.dma_start(W[:, 0, :], weight[0:P, :]).then_inc(weight_loaded[0], 16)
            for j in range(len(MAIN_TILES)):
                if j >= RING:
                    sp.wait_ge(summed, last_step(MAIN_TILES, j - RING))
                load_tile(0, MAIN_TILES, j, j % RING)
                if j == 0:
                    sp.dma_start(b_coef[0:N, :], column(scale)).then_inc(bias_loaded, 16)
                    sp.dma_start(bscale_col[:, :], column(bscale)).then_inc(bias_loaded, 16)
                    sp.dma_start(zp_col[:, :], column(zp)).then_inc(bias_loaded, 16)
                    sp.dma_start(bq_rows[:, :], bq).then_inc(bias_loaded, 16)
                    sp.dma_start(b_rows[N:N + 1, :], bias.rearrange("(a n) -> a n", a=1)
                                 ).then_inc(bias_loaded, 16)
                if j % 2:
                    n = j // 2
                    if n:
                        sp.wait_ge(x_turned, n * X_TILE)
                    sp.dma_start(xs[:, :, :], x_rows[:, n * X_TILE:(n + 1) * X_TILE, :]
                                 ).then_inc(x_loaded, 16)
            sp.dma_start(W[:, 1, :], weight[P:2 * P, :]).then_inc(weight_loaded[1], 16)
            with sp.Fori(1, MAIN) as b:
                for j in range(len(MAIN_TILES)):
                    if j >= RING:
                        sp.wait_ge(summed, b * MAIN_STEPS + last_step(MAIN_TILES, j - RING))
                    else:
                        sp.wait_ge(summed, b * MAIN_STEPS - MAIN_STEPS
                                   + last_step(MAIN_TILES, len(MAIN_TILES) - RING + j))
                    load_tile(b * P, MAIN_TILES, j, j % RING)
            used = [(MAIN - 1) * MAIN_STEPS + last_step(MAIN_TILES, j) for j in range(len(MAIN_TILES))]
            for n, chunks in enumerate(TAIL_CUTS):
                tiles = cut(chunks, N)
                for j in range(len(tiles)):
                    g = tail_tile[n] + j
                    sp.wait_ge(summed, used[len(used) - RING])
                    load_tile((MAIN + n) * P, tiles, j, g % RING)
                    used.append(tail_step[n] + last_step(tiles, j, tail=True))
            for b in (NB - 3, NB - 2):
                sp.wait_ge(y_ready, (b + 1) * Q)
                sp.dma_start(out_rows[:, :, b * P:(b + 1) * P], y[:, b % 2, :, :]).then_inc(stored[b % 2], 16)
            for q in range(Q):
                sp.wait_ge(y_ready, (NB - 1) * Q + q + 1)
                sp.dma_start(out_rows[:, q * QT:(q + 1) * QT, (NB - 1) * P:], y_last[:, q * QT:(q + 1) * QT, :]
                             ).then_inc(last_stored, 16)
            for par in range(2):
                sp.wait_ge(stored[par], 16 * (NB // 2 - par))
            sp.wait_ge(last_stored, 16 * Q)

        @block.gpsimd
        def _(pool):
            nc.gpsimd.memset(ident[:, :], 0.0).then_inc(ident_zeroed, 1)
            pool.wait_ge(ident_zeroed, 1)
            nc.gpsimd.affine_select(out=ident[:, :], in_=ident[:, :], compare_op=ALU.not_equal, fill=1.0,
                                    base=0, pattern=[[-1, P]], channel_multiplier=1).then_inc(ident_ready, 1)

        @block.vector
        def _(dve):
            dve.wait_ge(coefs_loaded, 3 * 16)
            nc.vector.tensor_tensor(coef[:, :], scale_all[:, :], wscale_all[:, :], ALU.mult).then_inc(setup, 1)
            nc.vector.tensor_tensor(zp_terms[:, :], scale_all[:, :], zp_all[:, :], ALU.mult).then_inc(setup, 1)
            dve.wait_ge(setup, 2)
            nc.vector.reduce_sum(zp_sum[:, :], zp_terms[:, :], axis=AX.X).then_inc(setup, 1)
            dve.wait_ge(bias_loaded, 5 * 16)
            nc.vector.memset(b_coef[N:N + 1, :], 1.0).then_inc(b_rows_ready, 1)
            nc.vector.tensor_copy(zp_colf[:, :], zp_col[:, :]).then_inc(setup, 1)
            dve.wait_ge(setup, 4)
            nc.vector.tensor_scalar(b_rows[0:N, :], bq_rows[:, :], bscale_col[:, 0:1], zp_colf[:, 0:1],
                                    ALU.mult, ALU.add).then_inc(b_rows_ready, 1)
            dve.wait_ge(ident_ready, 1)

            def sum_block(par, loads, block_index, first_step, uses, tiles):
                dve.wait_ge(weight_loaded[par], 16 * loads)
                diag = W[:, par, bass.ds(block_index * P, P)]
                nc.vector.tensor_tensor(diag, diag, ident[:, :], ALU.add).then_inc(summed, 1)
                step = 1
                for j, (k0, kc, i0, ni) in enumerate(tiles):
                    s, use = uses(j)
                    dve.wait_ge(tile_loaded[s], 16 * use)
                    part = W[:, par, k0:k0 + kc]
                    for i in range(ni):
                        dve.wait_ge(summed, first_step + step)
                        nc.vector.scalar_tensor_tensor(
                            out=part, in0=tile_view(s, kc, ni)[:, i, :], scalar=coef[:, i0 + i:i0 + i + 1],
                            in1=part, op0=ALU.mult, op1=ALU.add).then_inc(summed, 1)
                        step += 1

            rounds = len(MAIN_TILES) // RING
            with dve.Fori(0, MAIN // 2) as pair:
                for par in range(2):
                    b = pair * 2 + par
                    sum_block(par, pair + 1, b, b * MAIN_STEPS,
                              lambda j, b=b: (j % RING, b * rounds + (j // RING + 1)), MAIN_TILES)

            def sum_tail_block(n):
                b, tiles = MAIN + n, cut(TAIL_CUTS[n], N)
                dve.wait_ge(weight_loaded[b % 2], 16 * (b // 2 + 1))
                diag = W[:, b % 2, b * P:(b + 1) * P]
                nc.vector.tensor_tensor(diag, diag, ident[:, :], ALU.add).then_inc(summed, 1)
                step = tail_step[n] + 1
                for j, (k0, kc, i0, ni) in enumerate(tiles):
                    g = tail_tile[n] + j
                    dve.wait_ge(tile_loaded[g % RING], 16 * (g // RING + 1))
                    part = W[:, b % 2, k0:k0 + kc]
                    for i in range(i0, i0 + ni):
                        ints = tile_view(g % RING, kc, ni)[:, i - i0, :]
                        dve.wait_ge(summed, step - 1 if i else step)
                        if i == 1:
                            nc.vector.tensor_scalar(odd[:, 0:kc], ints, coef[:, i:i + 1], None,
                                                    ALU.mult).then_inc(summed, 1)
                        else:
                            add_to = odd[:, 0:kc] if i % 2 else part
                            nc.vector.scalar_tensor_tensor(
                                out=add_to, in0=ints, scalar=coef[:, i:i + 1], in1=add_to,
                                op0=ALU.mult, op1=ALU.add).then_inc(summed, 1)
                        step += 1
                    if i0 + ni == N:
                        dve.wait_ge(summed, step)
                        nc.vector.tensor_tensor(part, part, odd[:, 0:kc], ALU.add).then_inc(summed, 1)
                        step += 1

            for n in range(TAIL):
                sum_tail_block(n)
            for q in range(Q):
                dve.wait_ge(y_turned, (NB - 1) * Q + q + 1)
                nc.vector.tensor_copy(y_last[:, q * QT:(q + 1) * QT, :],
                                      acc[:, q, :].rearrange("p (t o) -> p t o", o=P)).then_inc(y_ready, 1)

        @block.tensor
        def _(pe):
            pe.wait_ge(b_rows_ready, 2)
            for n in range(NB):
                mm = nc.tensor.matmul(acc[:, 0, n:n + 1], b_rows[:, n * P:(n + 1) * P], b_coef[:, :],
                                      start=True, stop=True)
            mm.then_inc(b_done, 1)
            pe.wait_ge(ident_ready, 1)
            for t in range(TT):
                if t % X_TILE == 0:
                    pe.wait_ge(x_loaded, 16 * (t // X_TILE + 1))
                if t >= 2:
                    pe.wait_ge(xT_ready, t - 1)
                for k in range(KT):
                    mm = nc.tensor.transpose(turn[:, t % 2, k * P:(k + 1) * P],
                                             xs[:, t % X_TILE, k * P:(k + 1) * P], ident[:, :])
                mm.then_inc(x_turned, 1)
            pe.wait_ge(xT_ready, TT)
            pe.wait_ge(b_ready, 1)

            def turn_back(q, b):
                pe.wait_ge(yT_ready, b * Q + q + 1)
                for t in range(QT):
                    mm = nc.tensor.transpose(acc[:, q, t * P:(t + 1) * P], yT[:, q, t * P:(t + 1) * P],
                                             ident[:, :])
                mm.then_inc(y_turned, 1)

            def product_block(par, b, first_step, first_chunk, chunks, first=False, chunk_steps=N):
                for c, (k0, kc, _) in enumerate(chunks):
                    pe.wait_ge(summed, first_step + 1 + chunk_steps * (c + 1))
                    k_tiles = range(k0 // P, (k0 + kc) // P)
                    for k in k_tiles:
                        mm = nc.tensor.transpose(turn[:, 0, k * P:(k + 1) * P],
                                                 W[:, par, k * P:(k + 1) * P], ident[:, :])
                    mm.then_inc(w_turned, 1)
                    pe.wait_ge(WT_ready, first_chunk + c + 1)
                    for q in range(Q):
                        if c == 0 and not first:
                            pe.wait_ge(y_ready, b * Q - Q + q + 1)
                        for k in k_tiles:
                            mm = nc.tensor.matmul(acc[:, q, :], WT[:, k, :], xT[:, k, q * BANK:(q + 1) * BANK],
                                                  start=(k == 0), stop=(k == KT - 1))
                        if c == len(chunks) - 1:
                            mm.then_inc(bank_done, 1)
                            if q:
                                turn_back(q - 1, b)
                turn_back(Q - 1, b)

            product_block(0, 0, 0, 0, MAIN_CUT, first=True)
            product_block(1, 1, MAIN_STEPS, 1, MAIN_CUT)
            with pe.Fori(1, MAIN // 2) as pair:
                for par in range(2):
                    b = pair * 2 + par
                    product_block(par, b, b * MAIN_STEPS, b, MAIN_CUT)
            for n, chunks in enumerate(TAIL_CUTS):
                b = MAIN + n
                product_block(b % 2, b, tail_step[n], tail_chunk[n], chunks,
                              chunk_steps=TAIL_CHUNK_STEPS)

        @block.scalar
        def _(act):
            def load_weight(row, par):
                act.dma_start(W[:, par, :], weight[bass.ds(row, P), :]).then_inc(weight_loaded[par], 16)

            act.wait_ge(b_done, 1)
            nc.scalar.copy(b_col[:, :], acc[:, 0, 0:NB]).then_inc(b_ready, 1)
            for t in range(TT):
                act.wait_ge(x_turned, t + 1)
                nc.scalar.copy(xT[:, :, t * P:(t + 1) * P],
                               turn[:, t % 2, :].rearrange("k (j p) -> k j p", p=P)).then_inc(xT_ready, 1)
            act.wait_ge(setup, 3)

            def finish_block(par, b, first_chunk, chunks, stores):
                for c, (k0, kc, _) in enumerate(chunks):
                    act.wait_ge(w_turned, first_chunk + c + 1)
                    if c == len(chunks) - 1 and stores is not None:
                        stores()
                    nc.scalar.activation(WT[:, k0 // P:(k0 + kc) // P, :],
                                         turn[:, 0, k0:k0 + kc].rearrange("k (j p) -> k j p", p=P),
                                         ACT.Identity, bias=zp_sum[:, 0:1]).then_inc(WT_ready, 1)

            def pick_bias(b, par):
                nc.scalar.copy(b_now[:, par:par + 1], b_col[:, bass.ds(b, 1)]).then_inc(b_now_ready, 1)

            def take_product(q, b, par):
                act.wait_ge(bank_done, b * Q + q + 1)
                nc.scalar.activation(yT[:, q, :], acc[:, q, :], ACT.Identity,
                                     bias=b_now[:, par:par + 1]).then_inc(yT_ready, 1)

            def take_result(q, b, par):
                act.wait_ge(y_turned, b * Q + q + 1)
                nc.scalar.copy(y[:, par, q * QT:(q + 1) * QT, :],
                               acc[:, q, :].rearrange("p (t o) -> p t o", o=P)).then_inc(y_ready, 1)

            def results(par, b, earlier_stores):
                pick_bias(b, par)
                act.wait_ge(b_now_ready, b + 1)
                take_product(0, b, par)
                if earlier_stores is not None:
                    act.wait_ge(stored[par], earlier_stores)
                for q in range(1, Q):
                    take_product(q, b, par)
                    take_result(q - 1, b, par)
                take_result(Q - 1, b, par)

            def store(b, par):
                act.wait_ge(y_ready, b * Q + Q)
                act.dma_start(out_rows[:, :, bass.ds(b * P, P)], y[:, par, :, :]).then_inc(stored[par], 16)

            def main_block(par, b, earlier_stores):
                finish_block(par, b, b, MAIN_CUT, lambda: load_weight(b * P + 2 * P, par))
                results(par, b, earlier_stores)

            main_block(0, 0, None)
            store(0, 0)
            main_block(1, 1, None)
            with act.Fori(1, MAIN // 2) as pair:
                store(pair * 2 - 1, 1)
                main_block(0, pair * 2, pair * 16)
                store(pair * 2, 0)
                main_block(1, pair * 2 + 1, pair * 16)
            finish_block(0, MAIN, tail_chunk[0], TAIL_CUTS[0], None)
            results(0, MAIN, 16 * (MAIN // 2))
            finish_block(1, MAIN + 1, tail_chunk[1], TAIL_CUTS[1], None)
            pick_bias(NB - 1, 1)
            act.wait_ge(b_now_ready, NB)
            for q in range(Q):
                take_product(q, NB - 1, 1)


_INS = ['x', 'condB_scale', 'itok_Bx4096x4096_0_255', 'condB_wscale', 'itok_Bx4096_0_255', 'condB_bscale',
        '_lenS', 'L0_cond_weight', 'L0_cond_bias']
_OUTS = [((32, 64, 1024), 'float32')]


def kernel(**inputs):
    import numpy as _np
    import concourse.bacc as _bacc
    from concourse import mybir as _mybir
    from concourse.bass_utils import run_bass_kernel_spmd as _run

    nc = _bacc.Bacc("TRN2", target_bir_lowering=False, num_devices=1)
    arrays, args = {}, []
    for name in _INS:
        a = _np.ascontiguousarray(inputs[name])
        arrays[f"in_{name}_dram"] = a
        args.append(nc.dram_tensor(f"in_{name}_dram", a.shape, _mybir.dt.from_np(a.dtype), kind="ExternalInput").ap())
    for i, (shape, dtype) in enumerate(_OUTS):
        dt = _mybir.dt.from_np(_np.dtype(dtype))
        args.append(nc.dram_tensor(f"out_{i}_dram", shape, dt, kind="ExternalOutput").ap())
    cond_linear_residual(nc, *args)
    r = _run(nc, [arrays], core_ids=[0])
    got = tuple(r.results[0][f"out_{i}_dram"] for i in range(len(_OUTS)))
    return got[0]
```

```python
from contextlib import ExitStack

import concourse.bass as bass
from concourse import mybir

ALU = mybir.AluOpType
ACT = mybir.ActivationFunctionType
AX = mybir.AxisListType
F32 = mybir.dt.float32
I32 = mybir.dt.int32

P = 128
BANK = 512
RING = 8
X_TILE = 4


def cut(chunks, adapters):
    return [(k0, kc, i0, ni) for k0, kc, ni in chunks for i0 in range(0, adapters, ni)]


def cond_linear_residual(nc: bass.Bass, x, scale, wq, wscale, bq, bscale, zp, weight, bias, out):
    N, OUT, IN = wq.shape
    TOK = x.shape[0] * x.shape[1]
    KT = IN // P
    TT = TOK // P
    QT = BANK // P
    Q = TT // QT
    NB = OUT // P
    TAIL = 2
    MAIN = NB - TAIL
    EARLY = 2
    assert MAIN % 2 == 0 and TAIL == 2 and Q == 4 and N % 32 == 0 and TAIL <= EARLY

    SLOT = 2 * IN
    MAIN_CUT = [(0, IN, SLOT // IN)]
    TAIL_CUTS = [
        [(0, IN // 2, 4), (IN // 2, IN // 2, 4)],
        [(0, IN // 2, 4), (IN // 2, 3 * IN // 8, 4), (7 * IN // 8, IN // 8, 8)],
    ]
    MAIN_TILES = cut(MAIN_CUT, N)
    assert len(MAIN_TILES) % RING == 0

    MAIN_STEPS = 1 + N
    TAIL_CHUNK_STEPS = N + 1

    tail_tile, tail_step, tail_chunk = [MAIN * len(MAIN_TILES)], [MAIN * MAIN_STEPS], [MAIN]
    for c in TAIL_CUTS:
        tail_tile.append(tail_tile[-1] + len(cut(c, N)))
        tail_step.append(tail_step[-1] + 1 + TAIL_CHUNK_STEPS * len(c))
        tail_chunk.append(tail_chunk[-1] + len(c))

    assert X_TILE * IN + 2 * OUT <= TT * MAIN * P

    x_rows = x.rearrange("b s k -> (b s) k").rearrange("(p t) k -> p t k", t=TT)
    out_rows = out.rearrange("b s o -> (b s) o").rearrange("(p t) o -> p t o", t=TT)

    ctx = ExitStack()
    with ctx:
        def sb(name, shape, dt=F32):
            return ctx.enter_context(nc.sbuf_tensor(name, shape, dt))

        def sem(name):
            return ctx.enter_context(nc.semaphore(name))

        ring = sb("ring", [P, RING, SLOT], I32)
        xT = sb("xT", [P, KT, TOK])
        W = sb("W", [P, 2, IN])
        odd = sb("odd", [P, IN // 2])
        WT = sb("WT", [P, KT, P])
        yT = sb("yT", [P, 2, BANK])
        y = sb("y", [P, TT, MAIN, P])
        ident = sb("ident", [P, P])
        scale_all = sb("scale_all", [P, N])
        wscale_all = sb("wscale_all", [P, N])
        zp_all = sb("zp_all", [P, N], I32)
        coef = sb("coef", [P, N])
        zp_terms = sb("zp_terms", [P, N])
        zp_sum = sb("zp_sum", [P, 1])
        bscale_col = sb("bscale_col", [N, 1])
        zp_col = sb("zp_col", [N, 1], I32)
        zp_colf = sb("zp_colf", [N, 1])
        b_coef = sb("b_coef", [N + 1, 1])
        b_col = sb("b_col", [P, NB])
        b_now = sb("b_now", [P, 2])

        acc = ctx.enter_context(nc.psum_tensor("acc", [P, Q, BANK], F32))
        turn = ctx.enter_context(nc.psum_tensor("turn", [P, 2, KT * P], F32))

        tile_loaded = [sem(f"tile_loaded{s}") for s in range(RING)]
        x_loaded = sem("x_loaded")
        weight_loaded = [sem(f"weight_loaded{s}") for s in range(2)]
        coefs_loaded = sem("coefs_loaded")
        bias_loaded = sem("bias_loaded")
        ident_zeroed = sem("ident_zeroed")
        ident_ready = sem("ident_ready")
        setup = sem("setup")
        b_rows_ready = sem("b_rows_ready")
        b_done = sem("b_done")
        b_now_ready = sem("b_now_ready")
        x_turned = sem("x_turned")
        xT_ready = sem("xT_ready")
        summed = sem("summed")
        w_turned = sem("w_turned")
        WT_ready = sem("WT_ready")
        bank_done = sem("bank_done")
        yT_ready = sem("yT_ready")
        y_turned = sem("y_turned")
        banks_free = sem("banks_free")
        early_stored = sem("early_stored")
        late_stored = sem("late_stored")

        block = ctx.enter_context(nc.Block())

        start_only = y[:, :, :, :].rearrange("p t s o -> p (t s o)")
        xs = start_only[:, 0:X_TILE * IN].rearrange("p (t k) -> p t k", k=IN)
        bias_rows = start_only[0:N + 1, X_TILE * IN:X_TILE * IN + 2 * OUT]
        b_rows = bias_rows[:, 0:OUT]
        bq_rows = bias_rows[0:N, OUT:2 * OUT].bitcast(I32)

        def y_bank(q, slot):
            return y[:, q * QT:(q + 1) * QT, bass.ds(slot, 1), :].rearrange("p t s o -> p t (s o)")

        def as_bank(q):
            return acc[:, q, :].rearrange("p (t o) -> p t o", o=P)

        def tile_view(s, kc, ni):
            return ring[:, s, 0:ni * kc].rearrange("p (i k) -> p i k", i=ni)

        def last_step(tiles, j, tail=False):
            added_up = sum(i0 + ni == N for _, _, i0, ni in tiles[:j]) if tail else 0
            return 1 + sum(ni for _, _, _, ni in tiles[:j + 1]) + added_up

        @block.sync
        def _(sp):
            def load_tile(row, tiles, j, s):
                k0, kc, i0, ni = tiles[j]
                sp.dma_start(tile_view(s, kc, ni),
                             wq[i0:i0 + ni, bass.ds(row, P), k0:k0 + kc].rearrange("i p k -> p i k")
                             ).then_inc(tile_loaded[s], 16)

            def everywhere(v):
                return v.rearrange("(a n) -> a n", a=1).to_broadcast([P, N])

            def column(v):
                return v.rearrange("(n a) -> n a", a=1)

            x_every = len(MAIN_TILES) // (TT // X_TILE)
            sp.dma_start(scale_all[:, :], everywhere(scale)).then_inc(coefs_loaded, 16)
            sp.dma_start(wscale_all[:, :], everywhere(wscale)).then_inc(coefs_loaded, 16)
            sp.dma_start(zp_all[:, :], everywhere(zp)).then_inc(coefs_loaded, 16)
            sp.dma_start(W[:, 0, :], weight[0:P, :]).then_inc(weight_loaded[0], 16)
            for j in range(len(MAIN_TILES)):
                if j >= RING:
                    sp.wait_ge(summed, last_step(MAIN_TILES, j - RING))
                load_tile(0, MAIN_TILES, j, j % RING)
                if j == 0:
                    sp.dma_start(b_coef[0:N, :], column(scale)).then_inc(bias_loaded, 16)
                    sp.dma_start(bscale_col[:, :], column(bscale)).then_inc(bias_loaded, 16)
                    sp.dma_start(zp_col[:, :], column(zp)).then_inc(bias_loaded, 16)
                    sp.dma_start(bq_rows[:, :], bq).then_inc(bias_loaded, 16)
                    sp.dma_start(b_rows[N:N + 1, :], bias.rearrange("(a n) -> a n", a=1)
                                 ).then_inc(bias_loaded, 16)
                if j % x_every == x_every - 1:
                    n = j // x_every
                    if n:
                        sp.wait_ge(x_turned, n * X_TILE)
                    sp.dma_start(xs[:, :, :], x_rows[:, n * X_TILE:(n + 1) * X_TILE, :]
                                 ).then_inc(x_loaded, 16)
            sp.dma_start(W[:, 1, :], weight[P:2 * P, :]).then_inc(weight_loaded[1], 16)
            with sp.Fori(1, MAIN) as b:
                for j in range(len(MAIN_TILES)):
                    if j >= RING:
                        sp.wait_ge(summed, b * MAIN_STEPS + last_step(MAIN_TILES, j - RING))
                    else:
                        sp.wait_ge(summed, b * MAIN_STEPS - MAIN_STEPS
                                   + last_step(MAIN_TILES, len(MAIN_TILES) - RING + j))
                    load_tile(b * P, MAIN_TILES, j, j % RING)
            used = [(MAIN - 1) * MAIN_STEPS + last_step(MAIN_TILES, j) for j in range(len(MAIN_TILES))]

            def store(b0, b1, stored):
                sp.wait_ge(banks_free, Q + b1 * Q)
                s0, s1 = b0 % MAIN, (b1 - 1) % MAIN + 1
                sp.dma_start(out_rows[:, :, b0 * P:b1 * P],
                             y[:, :, s0:s1, :].rearrange("p t s o -> p t (s o)")).then_inc(stored, 16)

            store(0, EARLY, early_stored)
            for n, chunks in enumerate(TAIL_CUTS):
                tiles = cut(chunks, N)
                for j in range(len(tiles)):
                    g = tail_tile[n] + j
                    sp.wait_ge(summed, used[len(used) - RING])
                    load_tile((MAIN + n) * P, tiles, j, g % RING)
                    used.append(tail_step[n] + last_step(tiles, j, tail=True))
            store(EARLY, MAIN, late_stored)
            store(MAIN, NB - 1, late_stored)
            for q in range(Q):
                sp.wait_ge(banks_free, Q + (NB - 1) * Q + q + 1)
                sp.dma_start(out_rows[:, q * QT:(q + 1) * QT, (NB - 1) * P:], y_bank(q, (NB - 1) % MAIN)
                             ).then_inc(late_stored, 16)
            sp.wait_ge(early_stored, 16)
            sp.wait_ge(late_stored, 16 * (2 + Q))

        @block.gpsimd
        def _(pool):
            nc.gpsimd.memset(ident[:, :], 0.0).then_inc(ident_zeroed, 1)
            pool.wait_ge(ident_zeroed, 1)
            nc.gpsimd.affine_select(out=ident[:, :], in_=ident[:, :], compare_op=ALU.not_equal, fill=1.0,
                                    base=0, pattern=[[-1, P]], channel_multiplier=1).then_inc(ident_ready, 1)

        @block.vector
        def _(dve):
            dve.wait_ge(coefs_loaded, 3 * 16)
            nc.vector.tensor_tensor(coef[:, :], scale_all[:, :], wscale_all[:, :], ALU.mult).then_inc(setup, 1)
            nc.vector.tensor_tensor(zp_terms[:, :], scale_all[:, :], zp_all[:, :], ALU.mult).then_inc(setup, 1)
            dve.wait_ge(setup, 2)
            nc.vector.reduce_sum(zp_sum[:, :], zp_terms[:, :], axis=AX.X).then_inc(setup, 1)
            dve.wait_ge(bias_loaded, 5 * 16)
            nc.vector.memset(b_coef[N:N + 1, :], 1.0).then_inc(b_rows_ready, 1)
            nc.vector.tensor_copy(zp_colf[:, :], zp_col[:, :]).then_inc(setup, 1)
            dve.wait_ge(setup, 4)
            nc.vector.tensor_scalar(b_rows[0:N, :], bq_rows[:, :], bscale_col[:, 0:1], zp_colf[:, 0:1],
                                    ALU.mult, ALU.add).then_inc(b_rows_ready, 1)
            dve.wait_ge(ident_ready, 1)

            def sum_block(par, loads, block_index, first_step, uses, tiles):
                dve.wait_ge(weight_loaded[par], 16 * loads)
                diag = W[:, par, bass.ds(block_index * P, P)]
                nc.vector.tensor_tensor(diag, diag, ident[:, :], ALU.add).then_inc(summed, 1)
                step = 1
                for j, (k0, kc, i0, ni) in enumerate(tiles):
                    s, use = uses(j)
                    dve.wait_ge(tile_loaded[s], 16 * use)
                    part = W[:, par, k0:k0 + kc]
                    for i in range(ni):
                        dve.wait_ge(summed, first_step + step)
                        nc.vector.scalar_tensor_tensor(
                            out=part, in0=tile_view(s, kc, ni)[:, i, :], scalar=coef[:, i0 + i:i0 + i + 1],
                            in1=part, op0=ALU.mult, op1=ALU.add).then_inc(summed, 1)
                        step += 1

            rounds = len(MAIN_TILES) // RING
            with dve.Fori(0, MAIN // 2) as pair:
                for par in range(2):
                    b = pair * 2 + par
                    sum_block(par, pair + 1, b, b * MAIN_STEPS,
                              lambda j, b=b: (j % RING, b * rounds + (j // RING + 1)), MAIN_TILES)

            def sum_tail_block(n):
                b, tiles = MAIN + n, cut(TAIL_CUTS[n], N)
                dve.wait_ge(weight_loaded[b % 2], 16 * (b // 2 + 1))
                diag = W[:, b % 2, b * P:(b + 1) * P]
                nc.vector.tensor_tensor(diag, diag, ident[:, :], ALU.add).then_inc(summed, 1)
                step = tail_step[n] + 1
                for j, (k0, kc, i0, ni) in enumerate(tiles):
                    g = tail_tile[n] + j
                    dve.wait_ge(tile_loaded[g % RING], 16 * (g // RING + 1))
                    part = W[:, b % 2, k0:k0 + kc]
                    for i in range(i0, i0 + ni):
                        ints = tile_view(g % RING, kc, ni)[:, i - i0, :]
                        dve.wait_ge(summed, step - 1 if i else step)
                        if i == 1:
                            nc.vector.tensor_scalar(odd[:, 0:kc], ints, coef[:, i:i + 1], None,
                                                    ALU.mult).then_inc(summed, 1)
                        else:
                            add_to = odd[:, 0:kc] if i % 2 else part
                            nc.vector.scalar_tensor_tensor(
                                out=add_to, in0=ints, scalar=coef[:, i:i + 1], in1=add_to,
                                op0=ALU.mult, op1=ALU.add).then_inc(summed, 1)
                        step += 1
                    if i0 + ni == N:
                        dve.wait_ge(summed, step)
                        nc.vector.tensor_tensor(part, part, odd[:, 0:kc], ALU.add).then_inc(summed, 1)
                        step += 1

            for n in range(TAIL):
                sum_tail_block(n)
            dve.wait_ge(early_stored, 16)
            for q in range(Q):
                dve.wait_ge(y_turned, (NB - 1) * Q + q + 1)
                nc.vector.tensor_copy(y_bank(q, (NB - 1) % MAIN), as_bank(q)).then_inc(banks_free, 1)

        @block.tensor
        def _(pe):
            pe.wait_ge(b_rows_ready, 2)
            for n in range(NB):
                mm = nc.tensor.matmul(acc[:, 0, n:n + 1], b_rows[:, n * P:(n + 1) * P], b_coef[:, :],
                                      start=True, stop=True)
            mm.then_inc(b_done, 1)
            pe.wait_ge(ident_ready, 1)
            for t in range(TT):
                if t % X_TILE == 0:
                    pe.wait_ge(x_loaded, 16 * (t // X_TILE + 1))
                if t >= 2:
                    pe.wait_ge(xT_ready, t - 1)
                for k in range(KT):
                    mm = nc.tensor.transpose(turn[:, t % 2, k * P:(k + 1) * P],
                                             xs[:, t % X_TILE, k * P:(k + 1) * P], ident[:, :])
                mm.then_inc(x_turned, 1)
            pe.wait_ge(xT_ready, TT)

            def turn_back(q, b):
                pe.wait_ge(yT_ready, b * Q + q + 1)
                for t in range(QT):
                    mm = nc.tensor.transpose(acc[:, q, t * P:(t + 1) * P], yT[:, q % 2, t * P:(t + 1) * P],
                                             ident[:, :])
                mm.then_inc(y_turned, 1)

            def product_block(par, b, first_step, first_chunk, chunks, chunk_steps=N):
                for c, (k0, kc, _) in enumerate(chunks):
                    pe.wait_ge(summed, first_step + 1 + chunk_steps * (c + 1))
                    k_tiles = range(k0 // P, (k0 + kc) // P)
                    for k in k_tiles:
                        mm = nc.tensor.transpose(turn[:, 0, k * P:(k + 1) * P],
                                                 W[:, par, k * P:(k + 1) * P], ident[:, :])
                    mm.then_inc(w_turned, 1)
                    pe.wait_ge(WT_ready, first_chunk + c + 1)
                    for q in range(Q):
                        if c == 0:
                            pe.wait_ge(banks_free, b * Q + q + 1)
                        for k in k_tiles:
                            mm = nc.tensor.matmul(acc[:, q, :], WT[:, k, :], xT[:, k, q * BANK:(q + 1) * BANK],
                                                  start=(k == 0), stop=(k == KT - 1))
                        if c == len(chunks) - 1:
                            mm.then_inc(bank_done, 1)
                            if q:
                                turn_back(q - 1, b)
                turn_back(Q - 1, b)

            with pe.Fori(0, MAIN // 2) as pair:
                for par in range(2):
                    b = pair * 2 + par
                    product_block(par, b, b * MAIN_STEPS, b, MAIN_CUT)
            for n, chunks in enumerate(TAIL_CUTS):
                b = MAIN + n
                product_block(b % 2, b, tail_step[n], tail_chunk[n], chunks,
                              chunk_steps=TAIL_CHUNK_STEPS)

        @block.scalar
        def _(act):
            def load_weight(row, par):
                act.dma_start(W[:, par, :], weight[bass.ds(row, P), :]).then_inc(weight_loaded[par], 16)

            act.wait_ge(b_done, 1)
            nc.scalar.copy(b_col[:, :], acc[:, 0, 0:NB]).then_inc(banks_free, Q)
            for t in range(TT):
                act.wait_ge(x_turned, t + 1)
                nc.scalar.copy(xT[:, :, t * P:(t + 1) * P],
                               turn[:, t % 2, :].rearrange("k (j p) -> k j p", p=P)).then_inc(xT_ready, 1)
            act.wait_ge(setup, 3)

            def finish_block(par, b, first_chunk, chunks, stores):
                for c, (k0, kc, _) in enumerate(chunks):
                    act.wait_ge(w_turned, first_chunk + c + 1)
                    if c == len(chunks) - 1 and stores is not None:
                        stores()
                    nc.scalar.activation(WT[:, k0 // P:(k0 + kc) // P, :],
                                         turn[:, 0, k0:k0 + kc].rearrange("k (j p) -> k j p", p=P),
                                         ACT.Identity, bias=zp_sum[:, 0:1]).then_inc(WT_ready, 1)

            def pick_bias(b, par):
                nc.scalar.copy(b_now[:, par:par + 1], b_col[:, bass.ds(b, 1)]).then_inc(b_now_ready, 1)

            def take_product(q, b, par):
                act.wait_ge(bank_done, b * Q + q + 1)
                nc.scalar.activation(yT[:, q % 2, :], acc[:, q, :], ACT.Identity,
                                     bias=b_now[:, par:par + 1]).then_inc(yT_ready, 1)

            def take_result(q, b, slot):
                act.wait_ge(y_turned, b * Q + q + 1)
                nc.scalar.copy(y_bank(q, slot), as_bank(q)).then_inc(banks_free, 1)

            def results(par, b, slot):
                pick_bias(b, par)
                act.wait_ge(b_now_ready, b + 1)
                take_product(0, b, par)
                for q in range(1, Q):
                    take_product(q, b, par)
                    take_result(q - 1, b, slot)
                take_result(Q - 1, b, slot)

            with act.Fori(0, MAIN // 2) as pair:
                for par in range(2):
                    b = pair * 2 + par
                    finish_block(par, b, b, MAIN_CUT, lambda b=b, par=par: load_weight(b * P + 2 * P, par))
                    results(par, b, b)
            finish_block(0, MAIN, tail_chunk[0], TAIL_CUTS[0], None)
            act.wait_ge(early_stored, 16)
            results(0, MAIN, 0)
            finish_block(1, MAIN + 1, tail_chunk[1], TAIL_CUTS[1], None)
            pick_bias(NB - 1, 1)
            act.wait_ge(b_now_ready, NB)
            for q in range(Q):
                take_product(q, NB - 1, 1)


_INS = ['x', 'condB_scale', 'itok_Bx4096x4096_0_255', 'condB_wscale', 'itok_Bx4096_0_255', 'condB_bscale',
        '_lenS', 'L0_cond_weight', 'L0_cond_bias']
_OUTS = [((32, 64, 1024), 'float32')]


def kernel(**inputs):
    import numpy as _np
    import concourse.bacc as _bacc
    from concourse import mybir as _mybir
    from concourse.bass_utils import run_bass_kernel_spmd as _run

    nc = _bacc.Bacc("TRN2", target_bir_lowering=False, num_devices=1)
    arrays, args = {}, []
    for name in _INS:
        a = _np.ascontiguousarray(inputs[name])
        arrays[f"in_{name}_dram"] = a
        args.append(nc.dram_tensor(f"in_{name}_dram", a.shape, _mybir.dt.from_np(a.dtype), kind="ExternalInput").ap())
    for i, (shape, dtype) in enumerate(_OUTS):
        dt = _mybir.dt.from_np(_np.dtype(dtype))
        args.append(nc.dram_tensor(f"out_{i}_dram", shape, dt, kind="ExternalOutput").ap())
    cond_linear_residual(nc, *args)
    r = _run(nc, [arrays], core_ids=[0])
    got = tuple(r.results[0][f"out_{i}_dram"] for i in range(len(_OUTS)))
    return got[0]
```
